# Optimizing a Trainium2 kernel written in Bass

```python
import numpy as np
import jax
import jax.numpy as jnp

def _softmax(x, axis=-1):
    return jax.nn.softmax(x, axis=axis)

def _gelu(x):
    return jax.nn.gelu(x, approximate=True)

def _silu(x):
    return jax.nn.silu(x)

def _sigmoid(x):
    return jax.nn.sigmoid(x)

def _layernorm(x, axis=-1, eps=1e-05):
    m = jnp.mean(x, axis=axis, keepdims=True)
    v = jnp.var(x, axis=axis, keepdims=True)
    return (x - m) / jnp.sqrt(v + eps)

def _scatter_add(tgt, idx, src, axis=0):
    return tgt.at[idx].add(src)

def _segment_sum(src, seg, n):
    return jax.ops.segment_sum(src, seg, n)
kernel_name = 'mk_recurrent_d1_jaxref_r8_f11405'

def setup_inputs(seed: int=0):
    np.random.seed(seed)
    _w = jnp.asarray

    def _L0_attn_setup():
        import jax, jax.numpy as jnp
        import numpy as np
        from math import sqrt
        D_MODEL = 128
        B, T = (4, 512)
        key = jax.random.key(seed)
        kx, kqk, kvo = jax.random.split(key, 3)
        x = jax.random.normal(kx, (B, T, D_MODEL), dtype=jnp.float32)
        limit = sqrt(6.0 / (2 * D_MODEL))
        QK = jax.random.uniform(kqk, (D_MODEL, D_MODEL), minval=-limit, maxval=limit, dtype=jnp.float32)
        VO = jax.random.uniform(kvo, (D_MODEL, D_MODEL), minval=-limit, maxval=limit, dtype=jnp.float32)
        return {'x': x, 'QK': QK, 'VO': VO}
    _L0_attn_in = _L0_attn_setup()

    def _L0_ffn_setup():
        import jax, jax.numpy as jnp
        import numpy as np
        DIM = 128
        HIDDEN = 384
        SCALE = 1.0 / 127.0

        def _dequant(w_int, dtype):
            return w_int.astype(dtype) * jnp.asarray(SCALE, dtype)
        key = jax.random.key(seed)
        k_x, k_g, k_u, k_d = jax.random.split(key, 4)
        x = jax.random.normal(k_x, (4, 256, DIM), dtype=jnp.float32)
        w_gate = jax.random.randint(k_g, (HIDDEN, DIM), -127, 128, dtype=jnp.int32)
        w_up = jax.random.randint(k_u, (HIDDEN, DIM), -127, 128, dtype=jnp.int32)
        w_down = jax.random.randint(k_d, (DIM, HIDDEN), -127, 128, dtype=jnp.int32)
        return {'x': x, 'w_gate': w_gate, 'w_up': w_up, 'w_down': w_down}
    _L0_ffn_in = _L0_ffn_setup()
    _d = {'L0_attn_x': _L0_attn_in['x'], 'L0_attn_QK': _L0_attn_in['QK'], 'L0_attn_VO': _L0_attn_in['VO'], 'L0_ffn_w_gate': _L0_ffn_in['w_gate'], 'L0_ffn_w_up': _L0_ffn_in['w_up'], 'L0_ffn_w_down': _L0_ffn_in['w_down']}
    _x0 = _d['L0_attn_x']
    _d['L0_attn_x'] = jax.random.normal(jax.random.fold_in(jax.random.key(seed), 1), (16, 512, 128), dtype=_x0.dtype)
    del _x0
    return _d

def reference(L0_attn_x, L0_attn_QK, L0_attn_VO, L0_ffn_w_gate, L0_ffn_w_up, L0_ffn_w_down):

    def _L0_attn_ref(x, QK, VO):
        import jax, jax.numpy as jnp
        import numpy as np
        from math import sqrt
        D_MODEL = 128
        B, T = (4, 512)
        d_model = QK.shape[0]
        xQK = jnp.einsum('btd,de->bte', x, QK)
        scores = jnp.einsum('bte,bue->btu', xQK, x) / sqrt(d_model)
        attn = jax.nn.softmax(scores, axis=2)
        av = jnp.einsum('btu,bud->btd', attn, x)
        return jnp.einsum('btd,de->bte', av, VO)

    def _L0_ffn_ref(x, w_gate, w_up, w_down):
        import jax, jax.numpy as jnp
        import numpy as np
        DIM = 128
        HIDDEN = 384
        SCALE = 1.0 / 127.0

        def _dequant(w_int, dtype):
            return w_int.astype(dtype) * jnp.asarray(SCALE, dtype)
        wg = _dequant(w_gate, x.dtype)
        wu = _dequant(w_up, x.dtype)
        wd = _dequant(w_down, x.dtype)
        gate = jnp.einsum('bsd,hd->bsh', x, wg)
        up = jnp.einsum('bsd,hd->bsh', x, wu)
        h = jax.nn.silu(gate) * up
        return jnp.einsum('bsh,dh->bsd', h, wd)
    x = L0_attn_x
    xn = _layernorm(x, axis=-1)
    s = _L0_attn_ref(xn, L0_attn_QK, L0_attn_VO)
    g = _silu(_L0_ffn_ref(xn, L0_ffn_w_gate, L0_ffn_w_up, L0_ffn_w_down))
    x = x + s * g
    return x

_drawn_inputs = setup_inputs


def setup_inputs(seed=0):
    import zlib

    import numpy as np

    out = dict(_drawn_inputs(seed))
    spreads = {}
    factors = {}
    for name, (base, spread) in spreads.items():
        noise = np.random.default_rng([zlib.crc32(name.encode()), seed]).standard_normal(out[name].shape)
        drawn = base * np.exp(spread * noise) if base else spread * noise
        out[name] = jnp.asarray(drawn.astype(out[name].dtype))
    for name, factor in factors.items():
        out[name] = (out[name] * factor).astype(out[name].dtype)
    return out
```

```python
import concourse.bass as bass
from concourse import mybir
from contextlib import ExitStack

F32 = mybir.dt.float32
F32R = mybir.dt.float32r
I32 = mybir.dt.int32
ACT = mybir.ActivationFunctionType
ALU = mybir.AluOpType
AX = mybir.AxisListType


def gated_attention_kernel(nc: bass.Bass, x, qk, vo, w_gate_t, w_up_t, w_down_t, out):
    BATCHES, T, D = x.shape
    HIDDEN = w_gate_t.shape[1]
    P = 128
    TILES = T // P
    HT = HIDDEN // P
    PAIRS = BATCHES // 2
    EPS = 1e-5
    QSCALE = float(D) ** -0.5
    INT = 127.0
    TANH_GATE = 0.5 / INT
    TANH_OUT = 0.5 / (2 * INT ** 3)
    Y_SCALE = 1.0 / (4 * INT ** 3)

    x_v = x.rearrange("b (p i) d -> b p (i d)", i=TILES)
    out_v = out.rearrange("b (p i) d -> b p (i d)", i=TILES)

    with ExitStack() as ctx:
        def sb(name, shape, dt=F32):
            return ctx.enter_context(nc.sbuf_tensor(name, shape, dt))

        def bank(name):
            return ctx.enter_context(nc.psum_tensor(name, [P, 512], F32))

        def sem(name):
            return ctx.enter_context(nc.semaphore(name))

        def sems(name, n):
            return [sem(f"{name}{i}") for i in range(n)]

        ident = sb("ident", [P, P])
        eps = sb("eps", [P, TILES])
        minus_half = sb("minus_half", [P, TILES])
        ones = sb("ones", [P, 1])
        qk_f = sb("qk_f", [P, D])
        vo_f = sb("vo_f", [P, D])
        wg_i = sb("wg_i", [P, HIDDEN], I32)
        wu_i = sb("wu_i", [P, HIDDEN], I32)
        wd_i = sb("wd_i", [P, HT * D], I32)
        qk_hi, qk_lo = sb("qk_hi", [P, D], F32R), sb("qk_lo", [P, D], F32R)
        vo_hi, vo_lo = sb("vo_hi", [P, D], F32R), sb("vo_lo", [P, D], F32R)
        wg, wu = sb("wg", [P, HIDDEN], F32R), sb("wu", [P, HIDDEN], F32R)
        wd = sb("wd", [P, HT, D], F32R)

        x_all = sb("x_all", [P, BATCHES, TILES * D])
        stats = sb("stats", [P, 2, TILES, 6])
        mean_var = sb("mean_var", [P, 2, TILES, 2])
        var_eps = sb("var_eps", [P, TILES])
        rstd = sb("rstd", [P, TILES])
        xc = sb("xc", [P, TILES, D])
        xn = [sb(f"xn{p}", [P, TILES, D]) for p in range(2)]
        xT_hi = [sb(f"xT_hi{p}", [P, T], F32R) for p in range(2)]
        xT_lo = [sb(f"xT_lo{p}", [P, T], F32R) for p in range(2)]
        q_hi = [sb(f"q_hi{p}", [P, T], F32R) for p in range(2)]
        q_lo = [sb(f"q_lo{p}", [P, T], F32R) for p in range(2)]
        y = [sb(f"y{p}", [P, TILES, D]) for p in range(2)]
        neg_max = [sb(f"neg_max{p}", [P, TILES]) for p in range(2)]
        row_sum = [sb(f"row_sum{p}", [P, TILES]) for p in range(2)]
        recip = [sb(f"recip{p}", [P, TILES]) for p in range(2)]
        probs = [sb(f"probs{i}", [P, T]) for i in range(TILES)]
        probsT = [sb(f"probsT{p}", [P, TILES, T]) for p in range(2)]
        tanh_g = [sb(f"tanh_g{j}", [P, T]) for j in range(HT)]
        act_g = [sb(f"act_g{j}", [P, T]) for j in range(HT)]
        h = [sb(f"h{j}", [P, T]) for j in range(HT)]
        h_hi = [sb(f"h_hi{j}", [P, T], F32R) for j in range(HT)]
        h_lo = [sb(f"h_lo{j}", [P, T], F32R) for j in range(HT)]
        tanh_f = sb("tanh_f", [P, T])
        gT = sb("gT", [P, T])
        sgT = sb("sgT", [P, T])

        score_ps = [bank("score_ps0"), bank("score_ps1")]
        probsT_ps = [bank("probsT_ps0"), bank("probsT_ps1")]
        gate_ps, up_ps = bank("gate_ps"), bank("up_ps")
        front_ps = bank("front_ps")
        ffn_ps = bank("ffn_ps")

        const_ready, w_loaded, w_ready = sem("const_ready"), sem("w_loaded"), sem("w_ready")
        x_loaded, out_stored = sems("x_loaded", 2), sem("out_stored")
        stats_done, aggr_done = sem("stats_done"), sem("aggr_done")
        var_eps_done, rstd_done, xc_done, xn_ready = (
            sem("var_eps_done"), sem("rstd_done"), sem("xc_done"), sem("xn_ready"))
        xT_done, xT_hi_ready, xT_lo_ready = sem("xT_done"), sem("xT_hi_ready"), sem("xT_lo_ready")
        q_done, q_hi_ready, q_lo_ready = sem("q_done"), sem("q_hi_ready"), sem("q_lo_ready")
        y_done, y_ready = sem("y_done"), sem("y_ready")
        scores_done, max_done, exp_done = sems("scores_done", TILES), sems("max_done", TILES), sems("exp_done", TILES)
        probsT_done, probsT_ready = sems("probsT_done", TILES), sems("probsT_ready", TILES)
        recip_done = sem("recip_done")
        gate_up_done, tanh_done, act_done, h_done = (
            sems("gate_up_done", HT), sems("tanh_done", HT), sems("act_done", HT), sems("h_done", HT))
        h_hi_ready, h_lo_ready = sems("h_hi_ready", HT), sems("h_lo_ready", HT)
        attn_done, down_done = sem("attn_done"), sem("down_done")
        tanh_f_done, gT_done, sgT_done = sem("tanh_f_done"), sem("gT_done"), sem("sgT_done")
        back_done, final_done = sem("back_done"), sem("final_done")

        def run_batches(eng, step):
            for b in range(2):
                step(b, 0, b, b, False)
            with eng.Fori(1, PAIRS - 1) as pair:
                for p in range(2):
                    step(pair * 2 + p, pair, p, 2, False)
            for b in range(BATCHES - 2, BATCHES):
                step(b, PAIRS - 1, b % 2, 2, b == BATCHES - 1)

        block = ctx.enter_context(nc.Block())

        @block.sync
        def _(sp):
            sp.dma_start(x_all[:, 0, :], x_v[0]).then_inc(x_loaded[0], 16)
            sp.dma_start(qk_f[:, :], qk).then_inc(w_loaded, 16)
            sp.dma_start(vo_f[:, :], vo).then_inc(w_loaded, 16)
            sp.dma_start(wg_i[:, :], w_gate_t).then_inc(w_loaded, 16)
            sp.dma_start(wu_i[:, :], w_up_t).then_inc(w_loaded, 16)
            sp.dma_start(wd_i[:, :], w_down_t.rearrange("(j p) d -> p j d", p=P)).then_inc(w_loaded, 16)
            sp.dma_start(x_all[:, 1, :], x_v[1]).then_inc(x_loaded[1], 16)
            for pair in range(1, 2):
                for p in range(2):
                    sp.wait_ge(x_loaded[p], 16 * pair)
                    sp.dma_start(x_all[:, 2 * pair + p, :], x_v[2 * pair + p]).then_inc(x_loaded[p], 16)

            def store(b):
                sp.wait_ge(final_done, b + 1)
                sp.dma_start(out_v[b], x_all[:, b, :]).then_inc(out_stored, 16)

            with sp.Fori(0, PAIRS - 2) as pair:
                for p in range(2):
                    sp.wait_ge(x_loaded[p], pair * 16 + 32)
                    sp.dma_start(x_all[:, pair * 2 + (4 + p), :], x_v[pair * 2 + (4 + p)]).then_inc(x_loaded[p], 16)
                for p in range(2):
                    store(pair * 2 + p)
            for pair in range(PAIRS - 2, PAIRS):
                for p in range(2):
                    store(2 * pair + p)
            sp.wait_ge(out_stored, 16 * BATCHES)

        @block.gpsimd
        def _(pool):
            nc.gpsimd.memset(ident[:, :], 0.0).then_inc(const_ready, 1)
            nc.gpsimd.memset(eps[:, :], EPS)
            nc.gpsimd.memset(minus_half[:, :], -0.5)
            nc.gpsimd.memset(ones[:, :], 1.0).then_inc(const_ready, 1)
            pool.wait_ge(const_ready, 2)
            nc.gpsimd.affine_select(out=ident[:, :], in_=ident[:, :], compare_op=ALU.not_equal, fill=1.0,
                                    base=0, pattern=[[-1, P]], channel_multiplier=1).then_inc(const_ready, 1)

            def layernorm(n, p):
                pool.wait_ge(aggr_done, n + 1)
                nc.gpsimd.tensor_tensor(var_eps[:, :], mean_var[:, p, :, 1], eps[:, :], ALU.add).then_inc(var_eps_done, 1)
                x_b = x_all[:, n, :].rearrange("p (i d) -> p i d", i=TILES)
                nc.gpsimd.tensor_tensor(xc[:, :, :], x_b, mean_var[:, p, :, 0:1].to_broadcast([P, TILES, D]),
                                        ALU.subtract).then_inc(xc_done, 1)
                pool.wait_ge(var_eps_done, n + 1)
                nc.gpsimd.tensor_tensor(rstd[:, :], var_eps[:, :], minus_half[:, :], ALU.pow).then_inc(rstd_done, 1)
                pool.wait_ge(xc_done, n + 1)
                pool.wait_ge(rstd_done, n + 1)
                nc.gpsimd.tensor_tensor(xn[p][:, :, :], xc[:, :, :], rstd[:, :].unsqueeze(2).to_broadcast([P, TILES, D]),
                                        ALU.mult).then_inc(xn_ready, 1)

            def split_h(b, j, first):
                pool.wait_ge(h_done[j], b + 1)
                if not first:
                    pool.wait_ge(down_done, b)
                nc.gpsimd.tensor_tensor(h_hi[j][:, :], h[j][:, :], ones[:, 0:1].to_broadcast([P, T]),
                                        ALU.mult).then_inc(h_hi_ready[j], 1)
                pool.wait_ge(h_hi_ready[j], b + 1)
                nc.gpsimd.tensor_tensor(h_lo[j][:, :], h[j][:, :], h_hi[j][:, :].bitcast(F32),
                                        ALU.subtract).then_inc(h_lo_ready[j], 1)

            layernorm(0, 0)

            def step(b, pair, p, before, last):
                if not last:
                    layernorm(b + 1, 1 - p)
                for j in range(HT):
                    split_h(b, j, before == 0)

            run_batches(pool, step)

        @block.tensor
        def _(pe):
            def product(ps, parts, start=True, stop=True):
                for k, (lhsT, rhs) in enumerate(parts):
                    last = nc.tensor.matmul(ps, lhsT, rhs, start=start and k == 0, stop=stop and k == len(parts) - 1)
                return last

            def turn_x(n, p, first):
                pe.wait_ge(xn_ready, n + 1)
                if not first:
                    pe.wait_ge(sgT_done, n - 1)
                for i in range(TILES):
                    last = nc.tensor.transpose(front_ps[:, i * P:(i + 1) * P], xn[p][:, i, :], ident[:, :])
                last.then_inc(xT_done, 1)

            def project_q(n, p):
                pe.wait_ge(xT_lo_ready, n + 1)
                product(front_ps[:, :], [(qk_hi[:, :], xT_hi[p][:, :]), (qk_hi[:, :], xT_lo[p][:, :]),
                                         (qk_lo[:, :], xT_hi[p][:, :])]).then_inc(q_done, 1)

            def project_y(n, p, first):
                if not first:
                    pe.wait_ge(act_done[HT - 1], n)
                for i in range(TILES):
                    s = slice(i * P, (i + 1) * P)
                    last = product(gate_ps[:, s], [(xT_hi[p][:, s], vo_hi[:, :]), (xT_lo[p][:, s], vo_hi[:, :]),
                                                   (xT_hi[p][:, s], vo_lo[:, :])])
                last.then_inc(y_done, 1)

            def scores(b, p, i, first):
                if i == 0:
                    pe.wait_ge(q_lo_ready, b + 1)
                if i >= 2:
                    pe.wait_ge(exp_done[i - 2], b + 1)
                elif not first:
                    pe.wait_ge(exp_done[i + 2], b)
                s = slice(i * P, (i + 1) * P)
                product(score_ps[i % 2][:, :], [(q_hi[p][:, s], xT_hi[p][:, :]), (q_hi[p][:, s], xT_lo[p][:, :]),
                                                (q_lo[p][:, s], xT_hi[p][:, :])]).then_inc(scores_done[i], 1)

            def turn_probs(b, i, first):
                pe.wait_ge(exp_done[i], b + 1)
                if i >= 2:
                    pe.wait_ge(probsT_ready[i - 2], b + 1)
                elif not first:
                    pe.wait_ge(probsT_ready[i + 2], b)
                for k in range(TILES):
                    s = slice(k * P, (k + 1) * P)
                    last = nc.tensor.transpose(probsT_ps[i % 2][:, s], probs[i][:, s], ident[:, :])
                last.then_inc(probsT_done[i], 1)

            def gate_up(b, p, j, first):
                if j == 0:
                    pe.wait_ge(y_ready, b + 1)
                    if not first:
                        pe.wait_ge(h_done[HT - 1], b)
                else:
                    pe.wait_ge(h_done[j - 1], b + 1)
                s = slice(j * P, (j + 1) * P)
                product(gate_ps[:, :], [(wg[:, s], xT_hi[p][:, :]), (wg[:, s], xT_lo[p][:, :])])
                product(up_ps[:, :], [(wu[:, s], xT_hi[p][:, :]), (wu[:, s], xT_lo[p][:, :])]).then_inc(gate_up_done[j], 1)

            def attend(b, p, k):
                if k == 0:
                    for i in range(TILES):
                        pe.wait_ge(probsT_ready[i], b + 1)
                    pe.wait_ge(y_ready, b + 1)
                last = nc.tensor.matmul(front_ps[:, :], y[p][:, k, :], probsT[p][:, k, :],
                                        start=k == 0, stop=k == TILES - 1)
                if k == TILES - 1:
                    last.then_inc(attn_done, 1)

            def down(b, first):
                if not first:
                    pe.wait_ge(final_done, b)
                for j in range(HT):
                    pe.wait_ge(h_lo_ready[j], b + 1)
                    last = product(ffn_ps[:, :], [(wd[:, j, :], h_hi[j][:, :]), (wd[:, j, :], h_lo[j][:, :])],
                                   start=j == 0, stop=j == HT - 1)
                last.then_inc(down_done, 1)

            def turn_back(b):
                pe.wait_ge(sgT_done, b + 1)
                for i in range(TILES):
                    s = slice(i * P, (i + 1) * P)
                    last = nc.tensor.transpose(ffn_ps[:, s], sgT[:, s], ident[:, :])
                last.then_inc(back_done, 1)

            pe.wait_ge(const_ready, 3)
            turn_x(0, 0, True)
            pe.wait_ge(w_ready, 7)
            project_q(0, 0)
            project_y(0, 0, True)

            def step(b, pair, p, before, last):
                first = before == 0
                scores(b, p, 0, first)
                if not first:
                    attend(b - 1, 1 - p, 0)
                scores(b, p, 1, first)
                gate_up(b, p, 0, first)
                if not first:
                    attend(b - 1, 1 - p, 1)
                    down(b - 1, before == 1)
                turn_probs(b, 0, first)
                gate_up(b, p, 1, first)
                scores(b, p, 2, first)
                if not first:
                    attend(b - 1, 1 - p, 2)
                if not first:
                    attend(b - 1, 1 - p, 3)
                turn_probs(b, 1, first)
                scores(b, p, 3, first)
                if not last:
                    turn_x(b + 1, 1 - p, first)
                gate_up(b, p, 2, first)
                turn_probs(b, 2, first)
                if not first:
                    turn_back(b - 1)
                if not last:
                    project_q(b + 1, 1 - p)
                turn_probs(b, 3, first)
                if not last:
                    project_y(b + 1, 1 - p, False)

            run_batches(pe, step)
            for k in range(TILES):
                attend(BATCHES - 1, 1, k)
            down(BATCHES - 1, False)
            turn_back(BATCHES - 1)

        @block.scalar
        def _(act):
            def xT_part(n, p):
                act.wait_ge(xT_done, n + 1)
                nc.scalar.activation(xT_hi[p][:, :], front_ps[:, :], ACT.Copy).then_inc(xT_hi_ready, 1)

            def q_part(n, p):
                act.wait_ge(q_done, n + 1)
                nc.scalar.activation(q_hi[p][:, :], front_ps[:, :], ACT.Copy, scale=QSCALE).then_inc(q_hi_ready, 1)

            def y_copy(n, p):
                act.wait_ge(y_done, n + 1)
                nc.scalar.activation(y[p][:, :, :], gate_ps[:, :].rearrange("p (i d) -> p i d", i=TILES), ACT.Copy,
                                     scale=Y_SCALE).then_inc(y_ready, 1)

            def exp(b, p, i):
                act.wait_ge(max_done[i], b + 1)
                nc.scalar.activation(probs[i][:, :], score_ps[i % 2][:, :], ACT.Exp, bias=neg_max[p][:, i:i + 1],
                                     accum_out=row_sum[p][:, i:i + 1]).then_inc(exp_done[i], 1)

            def probsT_copy(b, p, i):
                act.wait_ge(probsT_done[i], b + 1)
                nc.scalar.activation(probsT[p][:, :, i * P:(i + 1) * P],
                                     probsT_ps[i % 2][:, :].rearrange("p (k t) -> p k t", k=TILES),
                                     ACT.Copy).then_inc(probsT_ready[i], 1)

            def tanh_gate(b, j):
                act.wait_ge(gate_up_done[j], b + 1)
                nc.scalar.activation(tanh_g[j][:, :], gate_ps[:, :], ACT.Tanh, scale=TANH_GATE).then_inc(tanh_done[j], 1)

            def tanh_ffn(b):
                act.wait_ge(down_done, b + 1)
                nc.scalar.activation(tanh_f[:, :], ffn_ps[:, :], ACT.Tanh, scale=TANH_OUT).then_inc(tanh_f_done, 1)

            xT_part(0, 0)
            q_part(0, 0)
            y_copy(0, 0)

            def step(b, pair, p, before, last):
                exp(b, p, 0)
                tanh_gate(b, 0)
                exp(b, p, 1)
                if before:
                    tanh_ffn(b - 1)
                probsT_copy(b, p, 0)
                tanh_gate(b, 1)
                exp(b, p, 2)
                probsT_copy(b, p, 1)
                if not last:
                    xT_part(b + 1, 1 - p)
                exp(b, p, 3)
                tanh_gate(b, 2)
                probsT_copy(b, p, 2)
                if not last:
                    q_part(b + 1, 1 - p)
                probsT_copy(b, p, 3)
                if not last:
                    y_copy(b + 1, 1 - p)

            run_batches(act, step)
            tanh_ffn(BATCHES - 1)

        @block.vector
        def _(dve):
            def statistics(n, p, x_pair):
                dve.wait_ge(x_loaded[p], x_pair * 16 + 16)
                for i in range(TILES):
                    last = nc.vector.bn_stats(stats[:, p, i, :], x_all[:, n, i * D:(i + 1) * D])
                last.then_inc(stats_done, 1)

            def wait_to_aggregate(n, first):
                dve.wait_ge(stats_done, n + 1)
                if not first:
                    dve.wait_ge(xn_ready, n - 1)

            def aggregate(p):
                for i in range(TILES):
                    last = nc.vector.bn_aggr(mean_var[:, p, i, :], stats[:, p, i, :])
                last.then_inc(aggr_done, 1)

            def xT_part(n, p):
                dve.wait_ge(xT_hi_ready, n + 1)
                nc.vector.tensor_tensor(xT_lo[p][:, :], front_ps[:, :], xT_hi[p][:, :].bitcast(F32),
                                        ALU.subtract).then_inc(xT_lo_ready, 1)

            def q_part(n, p):
                dve.wait_ge(q_hi_ready, n + 1)
                nc.vector.scalar_tensor_tensor(out=q_lo[p][:, :], in0=front_ps[:, :], scalar=QSCALE,
                                               in1=q_hi[p][:, :].bitcast(F32), op0=ALU.mult,
                                               op1=ALU.subtract).then_inc(q_lo_ready, 1)

            def row_max(b, p, i):
                dve.wait_ge(scores_done[i], b + 1)
                nc.vector.tensor_reduce(neg_max[p][:, i:i + 1], score_ps[i % 2][:, :], AX.X, ALU.max,
                                        negate=True).then_inc(max_done[i], 1)

            def gate(b, j):
                dve.wait_ge(tanh_done[j], b + 1)
                nc.vector.scalar_tensor_tensor(out=act_g[j][:, :], in0=tanh_g[j][:, :], scalar=1.0, in1=gate_ps[:, :],
                                               op0=ALU.add, op1=ALU.mult).then_inc(act_done[j], 1)

            def times_up(b, j, first):
                dve.wait_ge(act_done[j], b + 1)
                if not first:
                    dve.wait_ge(h_lo_ready[j], b)
                nc.vector.tensor_tensor(h[j][:, :], up_ps[:, :], act_g[j][:, :], ALU.mult).then_inc(h_done[j], 1)

            def gate_ffn(b):
                dve.wait_ge(tanh_f_done, b + 1)
                nc.vector.scalar_tensor_tensor(out=gT[:, :], in0=tanh_f[:, :], scalar=1.0, in1=ffn_ps[:, :],
                                               op0=ALU.add, op1=ALU.mult).then_inc(gT_done, 1)

            def times_attention(b, p):
                dve.wait_ge(attn_done, b + 1)
                dve.wait_ge(gT_done, b + 1)
                nc.vector.tensor_tensor(sgT[:, :], front_ps[:, :], gT[:, :], ALU.mult).then_inc(sgT_done, 1)

            def reciprocal(b, p):
                dve.wait_ge(exp_done[TILES - 1], b + 1)
                nc.vector.reciprocal(recip[p][:, :], row_sum[p][:, :]).then_inc(recip_done, 1)

            def finish(b, p):
                dve.wait_ge(back_done, b + 1)
                dve.wait_ge(recip_done, b + 1)
                for i in range(TILES):
                    s = slice(i * D, (i + 1) * D)
                    last = nc.vector.scalar_tensor_tensor(out=x_all[:, b, s], in0=ffn_ps[:, s], scalar=recip[p][:, i:i + 1],
                                                          in1=x_all[:, b, s], op0=ALU.mult, op1=ALU.add)
                last.then_inc(final_done, 1)

            statistics(0, 0, 0)
            wait_to_aggregate(0, True)
            aggregate(0)
            dve.wait_ge(w_loaded, 5 * 16)
            nc.vector.tensor_copy(qk_hi[:, :], qk_f[:, :]).then_inc(w_ready, 1)
            nc.vector.tensor_copy(vo_hi[:, :], vo_f[:, :]).then_inc(w_ready, 1)
            nc.vector.tensor_copy(wg[:, :], wg_i[:, :]).then_inc(w_ready, 1)
            nc.vector.tensor_copy(wu[:, :], wu_i[:, :]).then_inc(w_ready, 1)
            nc.vector.tensor_copy(wd[:, :, :], wd_i[:, :].rearrange("p (j d) -> p j d", j=HT)).then_inc(w_ready, 1)
            dve.wait_ge(w_ready, 2)
            nc.vector.tensor_tensor(qk_lo[:, :], qk_f[:, :], qk_hi[:, :].bitcast(F32), ALU.subtract).then_inc(w_ready, 1)
            nc.vector.tensor_tensor(vo_lo[:, :], vo_f[:, :], vo_hi[:, :].bitcast(F32), ALU.subtract).then_inc(w_ready, 1)
            xT_part(0, 0)
            q_part(0, 0)

            def step(b, pair, p, before, last):
                row_max(b, p, 0)
                if before == 2:
                    finish(b - 2, p)
                row_max(b, p, 1)
                if not last:
                    statistics(b + 1, 1 - p, pair + p)
                gate(b, 0)
                if not last:
                    wait_to_aggregate(b + 1, before == 0)
                times_up(b, 0, before == 0)
                if not last:
                    aggregate(1 - p)
                if before:
                    gate_ffn(b - 1)
                gate(b, 1)
                row_max(b, p, 2)
                times_up(b, 1, before == 0)
                if before:
                    times_attention(b - 1, 1 - p)
                row_max(b, p, 3)
                if not last:
                    xT_part(b + 1, 1 - p)
                gate(b, 2)
                reciprocal(b, p)
                times_up(b, 2, before == 0)
                if not last:
                    q_part(b + 1, 1 - p)

            run_batches(dve, step)
            finish(BATCHES - 2, 0)
            gate_ffn(BATCHES - 1)
            times_attention(BATCHES - 1, 1)
            finish(BATCHES - 1, 1)


def kernel(**inputs):
    import numpy as np
    import concourse.bacc as bacc
    from concourse.bass_utils import run_bass_kernel_spmd

    laid_out = {
        "x": np.asarray(inputs["L0_attn_x"]),
        "qk": np.asarray(inputs["L0_attn_QK"]),
        "vo": np.asarray(inputs["L0_attn_VO"]),
        "w_gate_t": np.asarray(inputs["L0_ffn_w_gate"]).T,
        "w_up_t": np.asarray(inputs["L0_ffn_w_up"]).T,
        "w_down_t": np.asarray(inputs["L0_ffn_w_down"]).T,
    }
    nc = bacc.Bacc("TRN2", target_bir_lowering=False, num_devices=1)
    arrays, args = {}, []
    for name, a in laid_out.items():
        a = np.ascontiguousarray(a)
        arrays[f"in_{name}"] = a
        args.append(nc.dram_tensor(f"in_{name}", a.shape, mybir.dt.from_np(a.dtype), kind="ExternalInput").ap())
    args.append(nc.dram_tensor("out_dram", laid_out["x"].shape, F32, kind="ExternalOutput").ap())
    gated_attention_kernel(nc, *args)
    return run_bass_kernel_spmd(nc, [arrays], core_ids=[0]).results[0]["out_dram"]
```

```python
import concourse.bass as bass
from concourse import mybir
from contextlib import ExitStack

F32 = mybir.dt.float32
F32R = mybir.dt.float32r
I32 = mybir.dt.int32
ACT = mybir.ActivationFunctionType
ALU = mybir.AluOpType
AX = mybir.AxisListType


def gated_attention_kernel(nc: bass.Bass, x, qk, vo, w_gate_t, w_up_t, w_down_t, out):
    BATCHES, T, D = x.shape
    HIDDEN = w_gate_t.shape[1]
    P = 128
    TILES = T // P
    HT = HIDDEN // P
    PAIRS = BATCHES // 2
    EPS = 1e-5
    QSCALE = float(D) ** -0.5
    INT = 127.0
    TANH_GATE = 0.5 / INT
    TANH_OUT = 0.5 / (2 * INT ** 3)
    AV_SCALE = 1.0 / (4 * INT ** 3)

    x_v = x.rearrange("b (p i) d -> b p (i d)", i=TILES)
    out_v = out.rearrange("b (p i) d -> b p (i d)", i=TILES)

    with ExitStack() as ctx:
        def sb(name, shape, dt=F32):
            return ctx.enter_context(nc.sbuf_tensor(name, shape, dt))

        def bank(name):
            return ctx.enter_context(nc.psum_tensor(name, [P, 512], F32))

        def sem(name):
            return ctx.enter_context(nc.semaphore(name))

        def sems(name, n):
            return [sem(f"{name}{i}") for i in range(n)]

        ident = sb("ident", [P, P])
        eps = sb("eps", [P, TILES])
        minus_half = sb("minus_half", [P, TILES])
        ones = sb("ones", [P, 1])
        qk_f = sb("qk_f", [P, D])
        vo_f = sb("vo_f", [P, D])
        wg_i = sb("wg_i", [P, HIDDEN], I32)
        wu_i = sb("wu_i", [P, HIDDEN], I32)
        wd_i = sb("wd_i", [P, HT * D], I32)
        qk_hi, qk_lo = sb("qk_hi", [P, D], F32R), sb("qk_lo", [P, D], F32R)
        vo_hi, vo_lo = sb("vo_hi", [P, D], F32R), sb("vo_lo", [P, D], F32R)
        wg, wu = sb("wg", [P, HIDDEN], F32R), sb("wu", [P, HIDDEN], F32R)
        wd = sb("wd", [P, HT, D], F32R)

        x_all = sb("x_all", [P, BATCHES, TILES * D])
        stats = sb("stats", [P, 2, TILES, 6])
        mean_var = sb("mean_var", [P, 2, TILES, 2])
        var_eps = sb("var_eps", [P, TILES])
        rstd = sb("rstd", [P, TILES])
        xc = sb("xc", [P, TILES, D])
        xn = [sb(f"xn{p}", [P, TILES, D]) for p in range(2)]
        xT_hi = [sb(f"xT_hi{p}", [P, T], F32R) for p in range(2)]
        xT_lo = [sb(f"xT_lo{p}", [P, T], F32R) for p in range(2)]
        q_hi = [sb(f"q_hi{p}", [P, T], F32R) for p in range(2)]
        q_lo = [sb(f"q_lo{p}", [P, T], F32R) for p in range(2)]
        xv_hi = [sb(f"xv_hi{p}", [P, TILES, D], F32R) for p in range(2)]
        xv_lo = [sb(f"xv_lo{p}", [P, TILES, D], F32R) for p in range(2)]
        neg_max = [sb(f"neg_max{p}", [P, TILES]) for p in range(2)]
        row_sum = [sb(f"row_sum{p}", [P, TILES]) for p in range(2)]
        recip = [sb(f"recip{p}", [P, TILES]) for p in range(2)]
        probs = [sb(f"probs{i}", [P, T]) for i in range(TILES)]
        probsT_hi = [sb(f"probsT_hi{p}", [P, TILES, T], F32R) for p in range(2)]
        probsT_lo = [sb(f"probsT_lo{p}", [P, TILES, T], F32R) for p in range(2)]
        av_hi, av_lo = sb("av_hi", [P, T], F32R), sb("av_lo", [P, T], F32R)
        tanh_g = [sb(f"tanh_g{j}", [P, T]) for j in range(HT)]
        act_g = [sb(f"act_g{j}", [P, T]) for j in range(HT)]
        h = [sb(f"h{j}", [P, T]) for j in range(HT)]
        h_hi = [[sb(f"h_hi{p}{j}", [P, T], F32R) for j in range(HT)] for p in range(2)]
        h_lo = [[sb(f"h_lo{p}{j}", [P, T], F32R) for j in range(HT)] for p in range(2)]
        tanh_f = sb("tanh_f", [P, T])
        gT = sb("gT", [P, T])
        sgT = sb("sgT", [P, T])
        scaled = sb("scaled", [P, TILES * D])

        score_ps = [bank("score_ps0"), bank("score_ps1")]
        probsT_ps = [bank("probsT_ps0"), bank("probsT_ps1")]
        gate_ps, up_ps = bank("gate_ps"), bank("up_ps")
        front_ps = bank("front_ps")
        ffn_ps = bank("ffn_ps")

        const_ready, w_loaded, w_ready = sem("const_ready"), sem("w_loaded"), sem("w_ready")
        x_loaded, out_stored = sems("x_loaded", 2), sem("out_stored")
        stats_done, aggr_done = sem("stats_done"), sem("aggr_done")
        var_eps_done, rstd_done, xc_done, xn_ready = (
            sem("var_eps_done"), sem("rstd_done"), sem("xc_done"), sem("xn_ready"))
        xT_done, xT_hi_ready, xT_lo_ready = sem("xT_done"), sem("xT_hi_ready"), sem("xT_lo_ready")
        q_done, q_hi_ready, q_lo_ready = sem("q_done"), sem("q_hi_ready"), sem("q_lo_ready")
        xv_hi_ready, xv_lo_ready = sem("xv_hi_ready"), sem("xv_lo_ready")
        scores_done, max_done, exp_done = sems("scores_done", TILES), sems("max_done", TILES), sems("exp_done", TILES)
        probsT_done, probsT_hi_ready, probsT_lo_ready = (
            sems("probsT_done", TILES), sems("probsT_hi_ready", TILES), sems("probsT_lo_ready", TILES))
        recip_done = sem("recip_done")
        gate_up_done, tanh_done, act_done, h_done = (
            sems("gate_up_done", HT), sems("tanh_done", HT), sems("act_done", HT), sems("h_done", HT))
        h_hi_ready, h_lo_ready = sems("h_hi_ready", HT), sems("h_lo_ready", HT)
        av_done, av_hi_ready, av_lo_ready = sem("av_done"), sem("av_hi_ready"), sem("av_lo_ready")
        attn_done, down_done = sem("attn_done"), sem("down_done")
        tanh_f_done, gT_done, sgT_done = sem("tanh_f_done"), sem("gT_done"), sem("sgT_done")
        back_done, scaled_done, final_done = sem("back_done"), sem("scaled_done"), sem("final_done")

        def live(b):
            return 0 <= b < BATCHES if isinstance(b, int) else True

        def later(b, n):
            return b >= n if isinstance(b, int) else True

        def run_steps(eng, step):
            for b in range(-1, 2):
                step(b, b // 2, b % 2)
            with eng.Fori(1, PAIRS - 1) as pair:
                for p in range(2):
                    step(pair * 2 + p, pair, p)
            for b in range(BATCHES - 2, BATCHES + 2):
                step(b, b // 2, b % 2)

        block = ctx.enter_context(nc.Block())

        @block.sync
        def _(sp):
            sp.dma_start(x_all[:, 0, :], x_v[0]).then_inc(x_loaded[0], 16)
            sp.dma_start(qk_f[:, :], qk).then_inc(w_loaded, 16)
            sp.dma_start(vo_f[:, :], vo).then_inc(w_loaded, 16)
            sp.dma_start(wg_i[:, :], w_gate_t).then_inc(w_loaded, 16)
            sp.dma_start(wu_i[:, :], w_up_t).then_inc(w_loaded, 16)
            sp.dma_start(wd_i[:, :], w_down_t.rearrange("(j p) d -> p j d", p=P)).then_inc(w_loaded, 16)
            sp.dma_start(x_all[:, 1, :], x_v[1]).then_inc(x_loaded[1], 16)
            for pair in range(1, 2):
                for p in range(2):
                    sp.wait_ge(x_loaded[p], 16 * pair)
                    sp.dma_start(x_all[:, 2 * pair + p, :], x_v[2 * pair + p]).then_inc(x_loaded[p], 16)

            def store(b):
                sp.wait_ge(final_done, b + 1)
                sp.dma_start(out_v[b], x_all[:, b, :]).then_inc(out_stored, 16)

            with sp.Fori(0, PAIRS - 2) as pair:
                for p in range(2):
                    sp.wait_ge(x_loaded[p], pair * 16 + 32)
                    sp.dma_start(x_all[:, pair * 2 + (4 + p), :], x_v[pair * 2 + (4 + p)]).then_inc(x_loaded[p], 16)
                for p in range(2):
                    store(pair * 2 + p)
            for pair in range(PAIRS - 2, PAIRS):
                for p in range(2):
                    store(2 * pair + p)
            sp.wait_ge(out_stored, 16 * BATCHES)

        @block.gpsimd
        def _(pool):
            nc.gpsimd.memset(ident[:, :], 0.0).then_inc(const_ready, 1)
            nc.gpsimd.memset(eps[:, :], EPS)
            nc.gpsimd.memset(minus_half[:, :], -0.5)
            nc.gpsimd.memset(ones[:, :], 1.0).then_inc(const_ready, 1)
            pool.wait_ge(const_ready, 2)
            nc.gpsimd.affine_select(out=ident[:, :], in_=ident[:, :], compare_op=ALU.not_equal, fill=1.0,
                                    base=0, pattern=[[-1, P]], channel_multiplier=1).then_inc(const_ready, 1)

            def layernorm(n, p):
                pool.wait_ge(aggr_done, n + 1)
                nc.gpsimd.tensor_tensor(var_eps[:, :], mean_var[:, p, :, 1], eps[:, :], ALU.add).then_inc(var_eps_done, 1)
                x_b = x_all[:, n, :].rearrange("p (i d) -> p i d", i=TILES)
                nc.gpsimd.tensor_tensor(xc[:, :, :], x_b, mean_var[:, p, :, 0:1].to_broadcast([P, TILES, D]),
                                        ALU.subtract).then_inc(xc_done, 1)
                pool.wait_ge(var_eps_done, n + 1)
                nc.gpsimd.tensor_tensor(rstd[:, :], var_eps[:, :], minus_half[:, :], ALU.pow).then_inc(rstd_done, 1)
                pool.wait_ge(xc_done, n + 1)
                pool.wait_ge(rstd_done, n + 1)
                nc.gpsimd.tensor_tensor(xn[p][:, :, :], xc[:, :, :], rstd[:, :].unsqueeze(2).to_broadcast([P, TILES, D]),
                                        ALU.mult).then_inc(xn_ready, 1)

            def xv_hi_part(b, p):
                pool.wait_ge(xn_ready, b + 1)
                if later(b, 2):
                    pool.wait_ge(av_done, b - 1)
                nc.gpsimd.tensor_tensor(xv_hi[p][:, :, :], xn[p][:, :, :],
                                        ones[:, 0:1].unsqueeze(2).to_broadcast([P, TILES, D]),
                                        ALU.mult).then_inc(xv_hi_ready, 1)

            def xv_lo_part(b, p):
                pool.wait_ge(xv_hi_ready, b + 1)
                nc.gpsimd.tensor_tensor(xv_lo[p][:, :, :], xn[p][:, :, :], xv_hi[p][:, :, :].bitcast(F32),
                                        ALU.subtract).then_inc(xv_lo_ready, 1)

            def h_part(b, p, j):
                pool.wait_ge(h_hi_ready[j], b + 1)
                nc.gpsimd.tensor_tensor(h_lo[p][j][:, :], h[j][:, :], h_hi[p][j][:, :].bitcast(F32),
                                        ALU.subtract).then_inc(h_lo_ready[j], 1)

            def add_x(b):
                pool.wait_ge(scaled_done, b + 1)
                nc.gpsimd.tensor_tensor(x_all[:, b, :], x_all[:, b, :], scaled[:, :], ALU.add).then_inc(final_done, 1)

            def step(b, pair, p):
                if live(b - 1):
                    h_part(b - 1, 1 - p, 2)
                    h_part(b - 1, 1 - p, 1)
                    h_part(b - 1, 1 - p, 0)
                if live(b + 1):
                    layernorm(b + 1, 1 - p)
                    xv_hi_part(b + 1, 1 - p)
                if live(b - 2):
                    add_x(b - 2)
                if live(b + 1):
                    xv_lo_part(b + 1, 1 - p)

            run_steps(pool, step)

        @block.tensor
        def _(pe):
            def product(ps, parts, start=True, stop=True):
                for k, (lhsT, rhs) in enumerate(parts):
                    last = nc.tensor.matmul(ps, lhsT, rhs, start=start and k == 0, stop=stop and k == len(parts) - 1)
                return last

            def turn_x(n, p):
                pe.wait_ge(xn_ready, n + 1)
                if later(n, 2):
                    pe.wait_ge(av_lo_ready, n - 1)
                for i in range(TILES):
                    last = nc.tensor.transpose(front_ps[:, i * P:(i + 1) * P], xn[p][:, i, :], ident[:, :])
                last.then_inc(xT_done, 1)

            def project_q(n, p):
                pe.wait_ge(xT_lo_ready, n + 1)
                product(front_ps[:, :], [(qk_hi[:, :], xT_hi[p][:, :]), (qk_hi[:, :], xT_lo[p][:, :]),
                                         (qk_lo[:, :], xT_hi[p][:, :])]).then_inc(q_done, 1)

            def scores(b, p, i):
                pe.wait_ge(q_lo_ready, b + 1)
                if i >= 2:
                    pe.wait_ge(exp_done[i - 2], b + 1)
                elif later(b, 1):
                    pe.wait_ge(exp_done[i + 2], b)
                s = slice(i * P, (i + 1) * P)
                product(score_ps[i % 2][:, :], [(q_hi[p][:, s], xT_hi[p][:, :]), (q_hi[p][:, s], xT_lo[p][:, :]),
                                                (q_lo[p][:, s], xT_hi[p][:, :])]).then_inc(scores_done[i], 1)

            def turn_probs(b, i):
                pe.wait_ge(exp_done[i], b + 1)
                if i >= 2:
                    pe.wait_ge(probsT_lo_ready[i - 2], b + 1)
                elif later(b, 1):
                    pe.wait_ge(probsT_lo_ready[i + 2], b)
                for k in range(TILES):
                    s = slice(k * P, (k + 1) * P)
                    last = nc.tensor.transpose(probsT_ps[i % 2][:, s], probs[i][:, s], ident[:, :])
                last.then_inc(probsT_done[i], 1)

            def gate_up(b, p, j):
                if j == 0:
                    pe.wait_ge(xT_lo_ready, b + 1)
                    if later(b, 1):
                        pe.wait_ge(h_done[HT - 1], b)
                else:
                    pe.wait_ge(h_done[j - 1], b + 1)
                s = slice(j * P, (j + 1) * P)
                product(gate_ps[:, :], [(wg[:, s], xT_hi[p][:, :]), (wg[:, s], xT_lo[p][:, :])])
                product(up_ps[:, :], [(wu[:, s], xT_hi[p][:, :]), (wu[:, s], xT_lo[p][:, :])]).then_inc(gate_up_done[j], 1)

            def attend(b, p, k):
                if k == 0:
                    for i in range(TILES):
                        pe.wait_ge(probsT_lo_ready[i], b + 1)
                    pe.wait_ge(xv_lo_ready, b + 1)
                    if live(b + 1):
                        pe.wait_ge(q_lo_ready, b + 2)
                last = product(front_ps[:, :], [(xv_hi[p][:, k, :], probsT_hi[p][:, k, :]),
                                                (xv_hi[p][:, k, :], probsT_lo[p][:, k, :]),
                                                (xv_lo[p][:, k, :], probsT_hi[p][:, k, :])],
                               start=k == 0, stop=k == TILES - 1)
                if k == TILES - 1:
                    last.then_inc(av_done, 1)

            def project_vo(b):
                pe.wait_ge(av_lo_ready, b + 1)
                pe.wait_ge(gT_done, b + 1)
                product(ffn_ps[:, :], [(vo_hi[:, :], av_hi[:, :]), (vo_hi[:, :], av_lo[:, :]),
                                       (vo_lo[:, :], av_hi[:, :])]).then_inc(attn_done, 1)

            def down(b, p, j):
                if j == 0 and later(b, 1):
                    pe.wait_ge(scaled_done, b)
                pe.wait_ge(h_lo_ready[j], b + 1)
                last = product(ffn_ps[:, :], [(wd[:, j, :], h_hi[p][j][:, :]), (wd[:, j, :], h_lo[p][j][:, :])],
                               start=j == 0, stop=j == HT - 1)
                if j == HT - 1:
                    last.then_inc(down_done, 1)

            def turn_back(b):
                pe.wait_ge(sgT_done, b + 1)
                for i in range(TILES):
                    s = slice(i * P, (i + 1) * P)
                    last = nc.tensor.transpose(ffn_ps[:, s], sgT[:, s], ident[:, :])
                last.then_inc(back_done, 1)

            pe.wait_ge(const_ready, 3)
            pe.wait_ge(w_ready, 7)

            def step(b, pair, p):
                if live(b):
                    turn_probs(b, 1)
                    gate_up(b, p, 1)
                    turn_probs(b, 0)
                if live(b - 1):
                    down(b - 1, 1 - p, 0)
                if live(b):
                    scores(b, p, 2)
                if live(b - 1):
                    down(b - 1, 1 - p, 1)
                if live(b + 1):
                    turn_x(b + 1, 1 - p)
                if live(b - 1):
                    down(b - 1, 1 - p, 2)
                if live(b):
                    gate_up(b, p, 2)
                    turn_probs(b, 3)
                if live(b + 1):
                    project_q(b + 1, 1 - p)
                if live(b - 1):
                    project_vo(b - 1)
                if live(b):
                    turn_probs(b, 2)
                if live(b + 1):
                    gate_up(b + 1, 1 - p, 0)
                if live(b - 1):
                    turn_back(b - 1)
                if live(b + 1):
                    scores(b + 1, 1 - p, 1)
                    scores(b + 1, 1 - p, 0)
                if live(b):
                    attend(b, p, 0)
                    attend(b, p, 1)
                    attend(b, p, 2)
                    attend(b, p, 3)
                if live(b + 1):
                    scores(b + 1, 1 - p, 3)

            run_steps(pe, step)

        @block.scalar
        def _(act):
            def xT_part(n, p):
                act.wait_ge(xT_done, n + 1)
                nc.scalar.activation(xT_hi[p][:, :], front_ps[:, :], ACT.Copy).then_inc(xT_hi_ready, 1)

            def q_part(n, p):
                act.wait_ge(q_done, n + 1)
                nc.scalar.activation(q_hi[p][:, :], front_ps[:, :], ACT.Copy, scale=QSCALE).then_inc(q_hi_ready, 1)

            def av_part(b):
                act.wait_ge(av_done, b + 1)
                nc.scalar.activation(av_hi[:, :], front_ps[:, :], ACT.Copy, scale=AV_SCALE).then_inc(av_hi_ready, 1)

            def h_part(b, p, j):
                act.wait_ge(h_done[j], b + 1)
                nc.scalar.activation(h_hi[p][j][:, :], h[j][:, :], ACT.Copy).then_inc(h_hi_ready[j], 1)

            def scale_rows(b, p):
                act.wait_ge(back_done, b + 1)
                act.wait_ge(recip_done, b + 1)
                if later(b, 1):
                    act.wait_ge(final_done, b)
                for i in range(TILES):
                    s = slice(i * D, (i + 1) * D)
                    last = nc.scalar.activation(scaled[:, s], ffn_ps[:, s], ACT.Copy, scale=recip[p][:, i:i + 1])
                last.then_inc(scaled_done, 1)

            def exp(b, p, i):
                act.wait_ge(max_done[i], b + 1)
                nc.scalar.activation(probs[i][:, :], score_ps[i % 2][:, :], ACT.Exp, bias=neg_max[p][:, i:i + 1],
                                     accum_out=row_sum[p][:, i:i + 1]).then_inc(exp_done[i], 1)

            def probsT_part(b, p, i):
                act.wait_ge(probsT_done[i], b + 1)
                nc.scalar.activation(probsT_hi[p][:, :, i * P:(i + 1) * P],
                                     probsT_ps[i % 2][:, :].rearrange("p (k t) -> p k t", k=TILES),
                                     ACT.Copy).then_inc(probsT_hi_ready[i], 1)

            def tanh_gate(b, j):
                act.wait_ge(gate_up_done[j], b + 1)
                nc.scalar.activation(tanh_g[j][:, :], gate_ps[:, :], ACT.Tanh, scale=TANH_GATE).then_inc(tanh_done[j], 1)

            def tanh_ffn(b):
                act.wait_ge(down_done, b + 1)
                nc.scalar.activation(tanh_f[:, :], ffn_ps[:, :], ACT.Tanh, scale=TANH_OUT).then_inc(tanh_f_done, 1)

            def step(b, pair, p):
                if live(b):
                    exp(b, p, 0)
                    probsT_part(b, p, 1)
                    tanh_gate(b, 1)
                    h_part(b, p, 0)
                    probsT_part(b, p, 0)
                    exp(b, p, 3)
                if live(b + 1):
                    xT_part(b + 1, 1 - p)
                if live(b - 1):
                    tanh_ffn(b - 1)
                if live(b):
                    tanh_gate(b, 2)
                    probsT_part(b, p, 3)
                    exp(b, p, 2)
                if live(b + 1):
                    q_part(b + 1, 1 - p)
                if live(b):
                    h_part(b, p, 2)
                    probsT_part(b, p, 2)
                    h_part(b, p, 1)
                if live(b + 1):
                    tanh_gate(b + 1, 0)
                if live(b - 1):
                    scale_rows(b - 1, 1 - p)
                if live(b + 1):
                    exp(b + 1, 1 - p, 1)
                if live(b):
                    av_part(b)

            run_steps(act, step)

        @block.vector
        def _(dve):
            def statistics(n, p, x_pair):
                dve.wait_ge(x_loaded[p], x_pair * 16 + 16)
                for i in range(TILES):
                    last = nc.vector.bn_stats(stats[:, p, i, :], x_all[:, n, i * D:(i + 1) * D])
                last.then_inc(stats_done, 1)

            def wait_to_aggregate(n):
                dve.wait_ge(stats_done, n + 1)
                if later(n, 2):
                    dve.wait_ge(xn_ready, n - 1)

            def aggregate(p):
                for i in range(TILES):
                    last = nc.vector.bn_aggr(mean_var[:, p, i, :], stats[:, p, i, :])
                last.then_inc(aggr_done, 1)

            def xT_part(n, p):
                dve.wait_ge(xT_hi_ready, n + 1)
                nc.vector.tensor_tensor(xT_lo[p][:, :], front_ps[:, :], xT_hi[p][:, :].bitcast(F32),
                                        ALU.subtract).then_inc(xT_lo_ready, 1)

            def q_part(n, p):
                dve.wait_ge(q_hi_ready, n + 1)
                nc.vector.scalar_tensor_tensor(out=q_lo[p][:, :], in0=front_ps[:, :], scalar=QSCALE,
                                               in1=q_hi[p][:, :].bitcast(F32), op0=ALU.mult,
                                               op1=ALU.subtract).then_inc(q_lo_ready, 1)

            def av_part(b):
                dve.wait_ge(av_hi_ready, b + 1)
                nc.vector.scalar_tensor_tensor(out=av_lo[:, :], in0=front_ps[:, :], scalar=AV_SCALE,
                                               in1=av_hi[:, :].bitcast(F32), op0=ALU.mult,
                                               op1=ALU.subtract).then_inc(av_lo_ready, 1)

            def probsT_part(b, p, i):
                dve.wait_ge(probsT_hi_ready[i], b + 1)
                s = slice(i * P, (i + 1) * P)
                nc.vector.tensor_tensor(probsT_lo[p][:, :, s], probsT_ps[i % 2][:, :].rearrange("p (k t) -> p k t", k=TILES),
                                        probsT_hi[p][:, :, s].bitcast(F32), ALU.subtract).then_inc(probsT_lo_ready[i], 1)

            def row_max(b, p, i):
                dve.wait_ge(scores_done[i], b + 1)
                nc.vector.tensor_reduce(neg_max[p][:, i:i + 1], score_ps[i % 2][:, :], AX.X, ALU.max,
                                        negate=True).then_inc(max_done[i], 1)

            def gate(b, j):
                dve.wait_ge(tanh_done[j], b + 1)
                nc.vector.scalar_tensor_tensor(out=act_g[j][:, :], in0=tanh_g[j][:, :], scalar=1.0, in1=gate_ps[:, :],
                                               op0=ALU.add, op1=ALU.mult).then_inc(act_done[j], 1)

            def times_up(b, j):
                dve.wait_ge(act_done[j], b + 1)
                if later(b, 1):
                    dve.wait_ge(h_lo_ready[j], b)
                nc.vector.tensor_tensor(h[j][:, :], up_ps[:, :], act_g[j][:, :], ALU.mult).then_inc(h_done[j], 1)

            def gate_ffn(b):
                dve.wait_ge(tanh_f_done, b + 1)
                nc.vector.scalar_tensor_tensor(out=gT[:, :], in0=tanh_f[:, :], scalar=1.0, in1=ffn_ps[:, :],
                                               op0=ALU.add, op1=ALU.mult).then_inc(gT_done, 1)

            def times_attention(b):
                dve.wait_ge(attn_done, b + 1)
                nc.vector.tensor_tensor(sgT[:, :], ffn_ps[:, :], gT[:, :], ALU.mult).then_inc(sgT_done, 1)

            def reciprocal(b, p):
                dve.wait_ge(exp_done[TILES - 1], b + 1)
                nc.vector.reciprocal(recip[p][:, :], row_sum[p][:, :]).then_inc(recip_done, 1)

            dve.wait_ge(w_loaded, 5 * 16)
            nc.vector.tensor_copy(qk_hi[:, :], qk_f[:, :]).then_inc(w_ready, 1)
            nc.vector.tensor_copy(vo_hi[:, :], vo_f[:, :]).then_inc(w_ready, 1)
            nc.vector.tensor_copy(wg[:, :], wg_i[:, :]).then_inc(w_ready, 1)
            nc.vector.tensor_copy(wu[:, :], wu_i[:, :]).then_inc(w_ready, 1)
            nc.vector.tensor_copy(wd[:, :, :], wd_i[:, :].rearrange("p (j d) -> p j d", j=HT)).then_inc(w_ready, 1)
            dve.wait_ge(w_ready, 2)
            nc.vector.tensor_tensor(qk_lo[:, :], qk_f[:, :], qk_hi[:, :].bitcast(F32), ALU.subtract).then_inc(w_ready, 1)
            nc.vector.tensor_tensor(vo_lo[:, :], vo_f[:, :], vo_hi[:, :].bitcast(F32), ALU.subtract).then_inc(w_ready, 1)
            def step(b, pair, p):
                if live(b):
                    q_part(b, p)
                if live(b - 1):
                    probsT_part(b - 1, 1 - p, 3)
                    probsT_part(b - 1, 1 - p, 2)
                if live(b + 1):
                    statistics(b + 1, 1 - p, pair + p)
                    wait_to_aggregate(b + 1)
                if live(b):
                    row_max(b, p, 1)
                if live(b + 1):
                    aggregate(1 - p)
                if live(b):
                    gate(b, 0)
                    row_max(b, p, 0)
                    times_up(b, 0)
                    row_max(b, p, 3)
                if live(b - 1):
                    av_part(b - 1)
                if live(b):
                    probsT_part(b, p, 1)
                    gate(b, 1)
                if live(b - 1):
                    reciprocal(b - 1, 1 - p)
                if live(b):
                    times_up(b, 1)
                    probsT_part(b, p, 0)
                    row_max(b, p, 2)
                if live(b + 1):
                    xT_part(b + 1, 1 - p)
                if live(b - 1):
                    gate_ffn(b - 1)
                if live(b):
                    gate(b, 2)
                    times_up(b, 2)
                if live(b - 1):
                    times_attention(b - 1)

            run_steps(dve, step)


def kernel(**inputs):
    import numpy as np
    import concourse.bacc as bacc
    from concourse.bass_utils import run_bass_kernel_spmd

    laid_out = {
        "x": np.asarray(inputs["L0_attn_x"]),
        "qk": np.asarray(inputs["L0_attn_QK"]),
        "vo": np.asarray(inputs["L0_attn_VO"]),
        "w_gate_t": np.asarray(inputs["L0_ffn_w_gate"]).T,
        "w_up_t": np.asarray(inputs["L0_ffn_w_up"]).T,
        "w_down_t": np.asarray(inputs["L0_ffn_w_down"]).T,
    }
    nc = bacc.Bacc("TRN2", target_bir_lowering=False, num_devices=1)
    arrays, args = {}, []
    for name, a in laid_out.items():
        a = np.ascontiguousarray(a)
        arrays[f"in_{name}"] = a
        args.append(nc.dram_tensor(f"in_{name}", a.shape, mybir.dt.from_np(a.dtype), kind="ExternalInput").ap())
    args.append(nc.dram_tensor("out_dram", laid_out["x"].shape, F32, kind="ExternalOutput").ap())
    gated_attention_kernel(nc, *args)
    return run_bass_kernel_spmd(nc, [arrays], core_ids=[0]).results[0]["out_dram"]
```

```python
import concourse.bass as bass
from concourse import mybir
from contextlib import ExitStack

F32 = mybir.dt.float32
F32R = mybir.dt.float32r
I32 = mybir.dt.int32
ACT = mybir.ActivationFunctionType
ALU = mybir.AluOpType
AX = mybir.AxisListType


def gated_attention_kernel(nc: bass.Bass, x, qk, vo, w_gate_t, w_up_t, w_down_t, out):
    BATCHES, T, D = x.shape
    HIDDEN = w_gate_t.shape[1]
    P = 128
    TILES = T // P
    HT = HIDDEN // P
    PAIRS = BATCHES // 2
    EPS = 1e-5
    QSCALE = float(D) ** -0.5
    INT = 127.0
    TANH_GATE = 0.5 / INT
    TANH_OUT = 0.5 / (2 * INT ** 3)
    AV_SCALE = 1.0 / (4 * INT ** 3)

    x_v = x.rearrange("b (p i) d -> b p (i d)", i=TILES)
    out_v = out.rearrange("b (p i) d -> b p (i d)", i=TILES)

    with ExitStack() as ctx:
        def sb(name, shape, dt=F32):
            return ctx.enter_context(nc.sbuf_tensor(name, shape, dt))

        def bank(name):
            return ctx.enter_context(nc.psum_tensor(name, [P, 512], F32))

        def sem(name):
            return ctx.enter_context(nc.semaphore(name))

        def sems(name, n):
            return [sem(f"{name}{i}") for i in range(n)]

        ident = sb("ident", [P, P])
        eps = sb("eps", [P, TILES])
        minus_half = sb("minus_half", [P, TILES])
        ones = sb("ones", [P, 1])
        qk_f = sb("qk_f", [P, D])
        vo_f = sb("vo_f", [P, D])
        wg_i = sb("wg_i", [P, HIDDEN], I32)
        wu_i = sb("wu_i", [P, HIDDEN], I32)
        wd_i = sb("wd_i", [P, HT * D], I32)
        qk_hi, qk_lo = sb("qk_hi", [P, D], F32R), sb("qk_lo", [P, D], F32R)
        vo_hi, vo_lo = sb("vo_hi", [P, D], F32R), sb("vo_lo", [P, D], F32R)
        wg, wu = sb("wg", [P, HIDDEN], F32R), sb("wu", [P, HIDDEN], F32R)
        wd = sb("wd", [P, HT, D], F32R)

        x_all = sb("x_all", [P, BATCHES, TILES * D])
        stats = sb("stats", [P, 2, TILES, 6])
        mean_var = sb("mean_var", [P, 2, TILES, 2])
        var_eps = sb("var_eps", [P, TILES])
        rstd = sb("rstd", [P, TILES])
        xc = sb("xc", [P, TILES, D])
        xn = [sb(f"xn{p}", [P, TILES, D]) for p in range(2)]
        xT_hi = [sb(f"xT_hi{p}", [P, T], F32R) for p in range(2)]
        xT_lo = [sb(f"xT_lo{p}", [P, T], F32R) for p in range(2)]
        q_hi = [sb(f"q_hi{p}", [P, T], F32R) for p in range(2)]
        q_lo = [sb(f"q_lo{p}", [P, T], F32R) for p in range(2)]
        xv_hi = [sb(f"xv_hi{p}", [P, TILES, D], F32R) for p in range(2)]
        xv_lo = [sb(f"xv_lo{p}", [P, TILES, D], F32R) for p in range(2)]
        neg_max = [sb(f"neg_max{p}", [P, TILES]) for p in range(2)]
        row_sum = [sb(f"row_sum{p}", [P, TILES]) for p in range(2)]
        recip = [sb(f"recip{p}", [P, TILES]) for p in range(2)]
        probs = [sb(f"probs{i}", [P, T]) for i in range(TILES)]
        probsT_hi = [sb(f"probsT_hi{p}", [P, TILES, T], F32R) for p in range(2)]
        probsT_lo = [sb(f"probsT_lo{p}", [P, TILES, T], F32R) for p in range(2)]
        av_hi, av_lo = sb("av_hi", [P, T], F32R), sb("av_lo", [P, T], F32R)
        tanh_g = [sb(f"tanh_g{j}", [P, T]) for j in range(HT)]
        act_g = [sb(f"act_g{j}", [P, T]) for j in range(HT)]
        h = [sb(f"h{j}", [P, T]) for j in range(HT)]
        h_hi = [[sb(f"h_hi{p}{j}", [P, T], F32R) for j in range(HT)] for p in range(2)]
        h_lo = [[sb(f"h_lo{p}{j}", [P, T], F32R) for j in range(HT)] for p in range(2)]
        tanh_f = sb("tanh_f", [P, T])
        gT = sb("gT", [P, T])
        sgT = sb("sgT", [P, T])
        scaled = sb("scaled", [P, TILES * D])

        score_ps = [bank("score_ps0"), bank("score_ps1")]
        probsT_ps = [bank("probsT_ps0"), bank("probsT_ps1")]
        gate_ps, up_ps = bank("gate_ps"), bank("up_ps")
        front_ps = bank("front_ps")
        ffn_ps = bank("ffn_ps")

        const_ready, ident_ready = sem("const_ready"), sem("ident_ready")
        attn_w_loaded, ffn_w_loaded = sem("attn_w_loaded"), sem("ffn_w_loaded")
        w_hi_ready, w_lo_ready = sem("w_hi_ready"), sem("w_lo_ready")
        x_loaded, out_stored = sems("x_loaded", 2), sem("out_stored")
        stats_done, aggr_done = sem("stats_done"), sem("aggr_done")
        var_eps_done, rstd_done, xc_done, xn_ready = (
            sem("var_eps_done"), sem("rstd_done"), sem("xc_done"), sem("xn_ready"))
        xT_done, xT_hi_ready, xT_lo_ready = sem("xT_done"), sem("xT_hi_ready"), sem("xT_lo_ready")
        q_done, q_hi_ready, q_lo_ready = sem("q_done"), sem("q_hi_ready"), sem("q_lo_ready")
        xv_hi_ready, xv_lo_ready = sem("xv_hi_ready"), sem("xv_lo_ready")
        scores_done, max_done, exp_done = sems("scores_done", TILES), sems("max_done", TILES), sems("exp_done", TILES)
        probsT_done, probsT_hi_ready, probsT_lo_ready = (
            sems("probsT_done", TILES), sems("probsT_hi_ready", TILES), sems("probsT_lo_ready", TILES))
        recip_done = sem("recip_done")
        gate_up_done, tanh_done, act_done, h_done = (
            sems("gate_up_done", HT), sems("tanh_done", HT), sems("act_done", HT), sems("h_done", HT))
        h_hi_ready, h_lo_ready = sems("h_hi_ready", HT), sems("h_lo_ready", HT)
        av_done, av_hi_ready, av_lo_ready = sem("av_done"), sem("av_hi_ready"), sem("av_lo_ready")
        attn_done, down_done = sem("attn_done"), sem("down_done")
        tanh_f_done, gT_done, sgT_done = sem("tanh_f_done"), sem("gT_done"), sem("sgT_done")
        back_done, scaled_done, final_done = sem("back_done"), sem("scaled_done"), sem("final_done")
        last_done = sem("last_done")

        def live(b):
            return 0 <= b < BATCHES if isinstance(b, int) else True

        def later(b, n):
            return b >= n if isinstance(b, int) else True

        def run_steps(eng, step):
            for b in range(-1, 2):
                step(b, b // 2, b % 2)
            with eng.Fori(1, PAIRS - 1) as pair:
                for p in range(2):
                    step(pair * 2 + p, pair, p)
            for b in range(BATCHES - 2, BATCHES + 2):
                step(b, b // 2, b % 2)

        block = ctx.enter_context(nc.Block())

        @block.sync
        def _(sp):
            sp.dma_start(x_all[:, 0, :], x_v[0]).then_inc(x_loaded[0], 16)
            sp.dma_start(qk_f[:, :], qk).then_inc(attn_w_loaded, 16)
            sp.dma_start(vo_f[:, :], vo).then_inc(attn_w_loaded, 16)
            sp.dma_start(wg_i[:, :], w_gate_t).then_inc(ffn_w_loaded, 16)
            sp.dma_start(wu_i[:, :], w_up_t).then_inc(ffn_w_loaded, 16)
            sp.dma_start(wd_i[:, :], w_down_t.rearrange("(j p) d -> p j d", p=P)).then_inc(ffn_w_loaded, 16)
            sp.dma_start(x_all[:, 1, :], x_v[1]).then_inc(x_loaded[1], 16)
            for p in range(2):
                sp.wait_ge(x_loaded[p], 16)
                sp.dma_start(x_all[:, 2 + p, :], x_v[2 + p]).then_inc(x_loaded[p], 16)

            def store(b):
                sp.wait_ge(final_done, b + 1)
                sp.dma_start(out_v[b], x_all[:, b, :]).then_inc(out_stored, 16)

            with sp.Fori(0, PAIRS - 2) as pair:
                for p in range(2):
                    sp.wait_ge(x_loaded[p], pair * 16 + 32)
                    sp.dma_start(x_all[:, pair * 2 + (4 + p), :], x_v[pair * 2 + (4 + p)]).then_inc(x_loaded[p], 16)
                for p in range(2):
                    store(pair * 2 + p)
            for b in range(BATCHES - 4, BATCHES - 1):
                store(b)
            for half in range(2):
                s = slice(half * TILES // 2 * D, (half + 1) * TILES // 2 * D)
                sp.wait_ge(last_done, half + 1)
                sp.dma_start(out_v[BATCHES - 1, :, s], x_all[:, BATCHES - 1, s]).then_inc(out_stored, 16)
            sp.wait_ge(out_stored, 16 * (BATCHES + 1))

        @block.gpsimd
        def _(pool):
            nc.gpsimd.memset(eps[:, :], EPS)
            nc.gpsimd.memset(minus_half[:, :], -0.5)
            nc.gpsimd.memset(ones[:, :], 1.0)
            nc.gpsimd.memset(ident[:, :], 0.0).then_inc(const_ready, 1)
            pool.wait_ge(const_ready, 1)
            nc.gpsimd.affine_select(out=ident[:, :], in_=ident[:, :], compare_op=ALU.not_equal, fill=1.0,
                                    base=0, pattern=[[-1, P]], channel_multiplier=1).then_inc(ident_ready, 1)

            def variance_plus_eps(n, p):
                pool.wait_ge(aggr_done, n + 1)
                nc.gpsimd.tensor_tensor(var_eps[:, :], mean_var[:, p, :, 1], eps[:, :], ALU.add).then_inc(var_eps_done, 1)

            def inverse_deviation(n):
                pool.wait_ge(var_eps_done, n + 1)
                nc.gpsimd.tensor_tensor(rstd[:, :], var_eps[:, :], minus_half[:, :], ALU.pow).then_inc(rstd_done, 1)

            def layernorm(n, p):
                variance_plus_eps(n, p)
                x_b = x_all[:, n, :].rearrange("p (i d) -> p i d", i=TILES)
                nc.gpsimd.tensor_tensor(xc[:, :, :], x_b, mean_var[:, p, :, 0:1].to_broadcast([P, TILES, D]),
                                        ALU.subtract).then_inc(xc_done, 1)
                inverse_deviation(n)
                pool.wait_ge(xc_done, n)
                pool.wait_ge(rstd_done, n + 1)
                nc.gpsimd.tensor_tensor(xn[p][:, :, :], xc[:, :, :], rstd[:, :].unsqueeze(2).to_broadcast([P, TILES, D]),
                                        ALU.mult).then_inc(xn_ready, 1)

            def xv_hi_part(b, p):
                pool.wait_ge(xn_ready, b + 1)
                if later(b, 2):
                    pool.wait_ge(av_done, b - 1)
                nc.gpsimd.tensor_tensor(xv_hi[p][:, :, :], xn[p][:, :, :],
                                        ones[:, 0:1].unsqueeze(2).to_broadcast([P, TILES, D]),
                                        ALU.mult).then_inc(xv_hi_ready, 1)

            def xv_lo_part(b, p):
                pool.wait_ge(xv_hi_ready, b + 1)
                nc.gpsimd.tensor_tensor(xv_lo[p][:, :, :], xn[p][:, :, :], xv_hi[p][:, :, :].bitcast(F32),
                                        ALU.subtract).then_inc(xv_lo_ready, 1)

            def h_part(b, p, j):
                pool.wait_ge(h_hi_ready[j], b + 1)
                nc.gpsimd.tensor_tensor(h_lo[p][j][:, :], h[j][:, :], h_hi[p][j][:, :].bitcast(F32),
                                        ALU.subtract).then_inc(h_lo_ready[j], 1)

            def add_x(b):
                pool.wait_ge(scaled_done, b + 1)
                nc.gpsimd.tensor_tensor(x_all[:, b, :], x_all[:, b, :], scaled[:, :], ALU.add).then_inc(final_done, 1)

            variance_plus_eps(0, 0)
            inverse_deviation(0)
            layernorm(1, 1)

            def step(b, pair, p):
                if live(b - 1):
                    xv_lo_part(b - 1, 1 - p)
                if live(b):
                    xv_hi_part(b, p)
                if live(b - 1):
                    h_part(b - 1, 1 - p, 2)
                    h_part(b - 1, 1 - p, 1)
                if live(b + 1) and later(b + 1, 2):
                    layernorm(b + 1, 1 - p)
                if live(b - 2) and live(b - 1):
                    add_x(b - 2)
                if live(b):
                    h_part(b, p, 0)

            run_steps(pool, step)

        @block.tensor
        def _(pe):
            def product(ps, parts, start=True, stop=True):
                for k, (lhsT, rhs) in enumerate(parts):
                    last = nc.tensor.matmul(ps, lhsT, rhs, start=start and k == 0, stop=stop and k == len(parts) - 1)
                return last

            def turn_x(n, p):
                pe.wait_ge(xn_ready, n + 1)
                if later(n, 2):
                    pe.wait_ge(av_lo_ready, n - 1)
                for i in range(TILES):
                    last = nc.tensor.transpose(front_ps[:, i * P:(i + 1) * P], xn[p][:, i, :], ident[:, :])
                last.then_inc(xT_done, 1)

            def project_q(n, p):
                pe.wait_ge(xT_lo_ready, n + 1)
                if not later(n, 1):
                    pe.wait_ge(w_lo_ready, 2)
                product(front_ps[:, :], [(qk_hi[:, :], xT_hi[p][:, :]), (qk_hi[:, :], xT_lo[p][:, :]),
                                         (qk_lo[:, :], xT_hi[p][:, :])]).then_inc(q_done, 1)

            def scores(b, p, i):
                pe.wait_ge(q_lo_ready, b + 1)
                if i >= 2:
                    pe.wait_ge(exp_done[i - 2], b + 1)
                elif later(b, 1):
                    pe.wait_ge(exp_done[i + 2], b)
                s = slice(i * P, (i + 1) * P)
                product(score_ps[i % 2][:, :], [(q_hi[p][:, s], xT_hi[p][:, :]), (q_hi[p][:, s], xT_lo[p][:, :]),
                                                (q_lo[p][:, s], xT_hi[p][:, :])]).then_inc(scores_done[i], 1)

            def turn_probs(b, i):
                pe.wait_ge(exp_done[i], b + 1)
                if i >= 2:
                    pe.wait_ge(probsT_lo_ready[i - 2], b + 1)
                elif later(b, 1):
                    pe.wait_ge(probsT_lo_ready[i + 2], b)
                for k in range(TILES):
                    s = slice(k * P, (k + 1) * P)
                    last = nc.tensor.transpose(probsT_ps[i % 2][:, s], probs[i][:, s], ident[:, :])
                last.then_inc(probsT_done[i], 1)

            def gate_up(b, p, j):
                if j == 0:
                    pe.wait_ge(xT_lo_ready, b + 1)
                    if later(b, 1):
                        pe.wait_ge(h_done[HT - 1], b)
                    else:
                        pe.wait_ge(w_hi_ready, 5)
                else:
                    pe.wait_ge(h_done[j - 1], b + 1)
                s = slice(j * P, (j + 1) * P)
                product(gate_ps[:, :], [(wg[:, s], xT_hi[p][:, :]), (wg[:, s], xT_lo[p][:, :])])
                product(up_ps[:, :], [(wu[:, s], xT_hi[p][:, :]), (wu[:, s], xT_lo[p][:, :])]).then_inc(gate_up_done[j], 1)

            def attend(b, p, k):
                if k == 0:
                    for i in range(TILES):
                        pe.wait_ge(probsT_lo_ready[i], b + 1)
                    pe.wait_ge(xv_lo_ready, b + 1)
                    if live(b + 1):
                        pe.wait_ge(q_lo_ready, b + 2)
                last = product(front_ps[:, :], [(xv_hi[p][:, k, :], probsT_hi[p][:, k, :]),
                                                (xv_hi[p][:, k, :], probsT_lo[p][:, k, :]),
                                                (xv_lo[p][:, k, :], probsT_hi[p][:, k, :])],
                               start=k == 0, stop=k == TILES - 1)
                if k == TILES - 1:
                    last.then_inc(av_done, 1)

            def project_vo(b):
                pe.wait_ge(av_lo_ready, b + 1)
                pe.wait_ge(gT_done, b + 1)
                product(ffn_ps[:, :], [(vo_hi[:, :], av_hi[:, :]), (vo_hi[:, :], av_lo[:, :]),
                                       (vo_lo[:, :], av_hi[:, :])]).then_inc(attn_done, 1)

            def down(b, p, j):
                if j == 0 and later(b, 1):
                    pe.wait_ge(scaled_done, b)
                pe.wait_ge(h_lo_ready[j], b + 1)
                last = product(ffn_ps[:, :], [(wd[:, j, :], h_hi[p][j][:, :]), (wd[:, j, :], h_lo[p][j][:, :])],
                               start=j == 0, stop=j == HT - 1)
                if j == HT - 1:
                    last.then_inc(down_done, 1)

            def turn_back(b):
                pe.wait_ge(sgT_done, b + 1)
                for i in range(TILES):
                    s = slice(i * P, (i + 1) * P)
                    last = nc.tensor.transpose(ffn_ps[:, s], sgT[:, s], ident[:, :])
                last.then_inc(back_done, 1)

            pe.wait_ge(ident_ready, 1)

            def step(b, pair, p):
                if live(b - 1):
                    attend(b - 1, 1 - p, 3)
                if live(b):
                    turn_probs(b, 1)
                    scores(b, p, 3)
                    gate_up(b, p, 2)
                    scores(b, p, 2)
                if live(b + 1):
                    turn_x(b + 1, 1 - p)
                if live(b):
                    turn_probs(b, 0)
                if live(b - 1):
                    down(b - 1, 1 - p, 0)
                if live(b):
                    turn_probs(b, 3)
                if live(b - 1):
                    down(b - 1, 1 - p, 1)
                    down(b - 1, 1 - p, 2)
                if live(b + 1):
                    project_q(b + 1, 1 - p)
                if live(b):
                    turn_probs(b, 2)
                if live(b + 1):
                    gate_up(b + 1, 1 - p, 0)
                if live(b - 1):
                    project_vo(b - 1)
                if live(b + 1):
                    scores(b + 1, 1 - p, 1)
                    scores(b + 1, 1 - p, 0)
                if live(b):
                    attend(b, p, 0)
                if live(b - 1):
                    turn_back(b - 1)
                if live(b + 1):
                    gate_up(b + 1, 1 - p, 1)
                if live(b):
                    attend(b, p, 1)
                    attend(b, p, 2)

            run_steps(pe, step)

        @block.scalar
        def _(act):
            def xT_part(n, p):
                act.wait_ge(xT_done, n + 1)
                nc.scalar.activation(xT_hi[p][:, :], front_ps[:, :], ACT.Copy).then_inc(xT_hi_ready, 1)

            def q_part(n, p):
                act.wait_ge(q_done, n + 1)
                nc.scalar.activation(q_hi[p][:, :], front_ps[:, :], ACT.Copy, scale=QSCALE).then_inc(q_hi_ready, 1)

            def av_part(b):
                act.wait_ge(av_done, b + 1)
                nc.scalar.activation(av_hi[:, :], front_ps[:, :], ACT.Copy, scale=AV_SCALE).then_inc(av_hi_ready, 1)

            def h_part(b, p, j):
                act.wait_ge(h_done[j], b + 1)
                nc.scalar.activation(h_hi[p][j][:, :], h[j][:, :], ACT.Copy).then_inc(h_hi_ready[j], 1)

            def scale_rows(b, p):
                act.wait_ge(back_done, b + 1)
                act.wait_ge(recip_done, b + 1)
                if later(b, 1):
                    act.wait_ge(final_done, b)
                for i in range(TILES):
                    s = slice(i * D, (i + 1) * D)
                    last = nc.scalar.activation(scaled[:, s], ffn_ps[:, s], ACT.Copy, scale=recip[p][:, i:i + 1])
                last.then_inc(scaled_done, 1)

            def exp(b, p, i):
                act.wait_ge(max_done[i], b + 1)
                nc.scalar.activation(probs[i][:, :], score_ps[i % 2][:, :], ACT.Exp, bias=neg_max[p][:, i:i + 1],
                                     accum_out=row_sum[p][:, i:i + 1]).then_inc(exp_done[i], 1)

            def probsT_part(b, p, i):
                act.wait_ge(probsT_done[i], b + 1)
                nc.scalar.activation(probsT_hi[p][:, :, i * P:(i + 1) * P],
                                     probsT_ps[i % 2][:, :].rearrange("p (k t) -> p k t", k=TILES),
                                     ACT.Copy).then_inc(probsT_hi_ready[i], 1)

            def tanh_gate(b, j):
                act.wait_ge(gate_up_done[j], b + 1)
                nc.scalar.activation(tanh_g[j][:, :], gate_ps[:, :], ACT.Tanh, scale=TANH_GATE).then_inc(tanh_done[j], 1)

            def tanh_ffn(b):
                act.wait_ge(down_done, b + 1)
                nc.scalar.activation(tanh_f[:, :], ffn_ps[:, :], ACT.Tanh, scale=TANH_OUT).then_inc(tanh_f_done, 1)

            act.wait_ge(attn_w_loaded, 2 * 16)
            nc.scalar.activation(qk_hi[:, :], qk_f[:, :], ACT.Copy).then_inc(w_hi_ready, 1)
            nc.scalar.activation(vo_hi[:, :], vo_f[:, :], ACT.Copy).then_inc(w_hi_ready, 1)
            act.wait_ge(ffn_w_loaded, 3 * 16)
            nc.scalar.activation(wg[:, :], wg_i[:, :], ACT.Copy).then_inc(w_hi_ready, 1)
            nc.scalar.activation(wu[:, :], wu_i[:, :], ACT.Copy).then_inc(w_hi_ready, 1)
            nc.scalar.activation(wd[:, :, :], wd_i[:, :].rearrange("p (j d) -> p j d", j=HT), ACT.Copy).then_inc(w_hi_ready, 1)

            def step(b, pair, p):
                if live(b):
                    exp(b, p, 0)
                if live(b - 1):
                    av_part(b - 1)
                if live(b):
                    probsT_part(b, p, 1)
                    h_part(b, p, 0)
                    tanh_gate(b, 2)
                    exp(b, p, 3)
                if live(b + 1):
                    xT_part(b + 1, 1 - p)
                if live(b):
                    probsT_part(b, p, 0)
                    exp(b, p, 2)
                    probsT_part(b, p, 3)
                if live(b - 1):
                    tanh_ffn(b - 1)
                if live(b + 1):
                    q_part(b + 1, 1 - p)
                if live(b):
                    probsT_part(b, p, 2)
                if live(b + 1):
                    tanh_gate(b + 1, 0)
                if live(b):
                    h_part(b, p, 2)
                    h_part(b, p, 1)
                if live(b - 1) and live(b):
                    scale_rows(b - 1, 1 - p)
                if live(b + 1):
                    tanh_gate(b + 1, 1)
                    exp(b + 1, 1 - p, 1)

            run_steps(act, step)

        @block.vector
        def _(dve):
            def statistics(n, p, x_pair):
                dve.wait_ge(x_loaded[p], x_pair * 16 + 16)
                for i in range(TILES):
                    last = nc.vector.bn_stats(stats[:, p, i, :], x_all[:, n, i * D:(i + 1) * D])
                last.then_inc(stats_done, 1)

            def wait_to_aggregate(n):
                dve.wait_ge(stats_done, n + 1)
                if later(n, 2):
                    dve.wait_ge(xn_ready, n - 1)

            def aggregate(p):
                for i in range(TILES):
                    last = nc.vector.bn_aggr(mean_var[:, p, i, :], stats[:, p, i, :])
                last.then_inc(aggr_done, 1)

            def xT_part(n, p):
                dve.wait_ge(xT_hi_ready, n + 1)
                nc.vector.tensor_tensor(xT_lo[p][:, :], front_ps[:, :], xT_hi[p][:, :].bitcast(F32),
                                        ALU.subtract).then_inc(xT_lo_ready, 1)

            def q_part(n, p):
                dve.wait_ge(q_hi_ready, n + 1)
                nc.vector.scalar_tensor_tensor(out=q_lo[p][:, :], in0=front_ps[:, :], scalar=QSCALE,
                                               in1=q_hi[p][:, :].bitcast(F32), op0=ALU.mult,
                                               op1=ALU.subtract).then_inc(q_lo_ready, 1)

            def av_part(b):
                dve.wait_ge(av_hi_ready, b + 1)
                nc.vector.scalar_tensor_tensor(out=av_lo[:, :], in0=front_ps[:, :], scalar=AV_SCALE,
                                               in1=av_hi[:, :].bitcast(F32), op0=ALU.mult,
                                               op1=ALU.subtract).then_inc(av_lo_ready, 1)

            def probsT_part(b, p, i):
                dve.wait_ge(probsT_hi_ready[i], b + 1)
                s = slice(i * P, (i + 1) * P)
                nc.vector.tensor_tensor(probsT_lo[p][:, :, s], probsT_ps[i % 2][:, :].rearrange("p (k t) -> p k t", k=TILES),
                                        probsT_hi[p][:, :, s].bitcast(F32), ALU.subtract).then_inc(probsT_lo_ready[i], 1)

            def row_max(b, p, i):
                dve.wait_ge(scores_done[i], b + 1)
                nc.vector.tensor_reduce(neg_max[p][:, i:i + 1], score_ps[i % 2][:, :], AX.X, ALU.max,
                                        negate=True).then_inc(max_done[i], 1)

            def gate(b, j):
                dve.wait_ge(tanh_done[j], b + 1)
                nc.vector.scalar_tensor_tensor(out=act_g[j][:, :], in0=tanh_g[j][:, :], scalar=1.0, in1=gate_ps[:, :],
                                               op0=ALU.add, op1=ALU.mult).then_inc(act_done[j], 1)

            def times_up(b, j):
                dve.wait_ge(act_done[j], b + 1)
                if later(b, 1):
                    dve.wait_ge(h_lo_ready[j], b)
                nc.vector.tensor_tensor(h[j][:, :], up_ps[:, :], act_g[j][:, :], ALU.mult).then_inc(h_done[j], 1)

            def gate_ffn(b):
                dve.wait_ge(tanh_f_done, b + 1)
                nc.vector.scalar_tensor_tensor(out=gT[:, :], in0=tanh_f[:, :], scalar=1.0, in1=ffn_ps[:, :],
                                               op0=ALU.add, op1=ALU.mult).then_inc(gT_done, 1)

            def times_attention(b):
                dve.wait_ge(attn_done, b + 1)
                nc.vector.tensor_tensor(sgT[:, :], ffn_ps[:, :], gT[:, :], ALU.mult).then_inc(sgT_done, 1)

            def reciprocal(b, p):
                dve.wait_ge(exp_done[TILES - 1], b + 1)
                nc.vector.reciprocal(recip[p][:, :], row_sum[p][:, :]).then_inc(recip_done, 1)

            statistics(0, 0, 0)
            wait_to_aggregate(0)
            aggregate(0)
            dve.wait_ge(w_hi_ready, 2)
            nc.vector.tensor_tensor(qk_lo[:, :], qk_f[:, :], qk_hi[:, :].bitcast(F32), ALU.subtract).then_inc(w_lo_ready, 1)
            nc.vector.tensor_tensor(vo_lo[:, :], vo_f[:, :], vo_hi[:, :].bitcast(F32), ALU.subtract).then_inc(w_lo_ready, 1)
            dve.wait_ge(rstd_done, 1)
            for i in range(TILES):
                last = nc.vector.tensor_scalar(xn[0][:, i, :], x_all[:, 0, i * D:(i + 1) * D], mean_var[:, 0, i, 0:1],
                                               rstd[:, i:i + 1], ALU.subtract, ALU.mult)
            last.then_inc(xn_ready, 1)
            statistics(1, 1, 0)
            wait_to_aggregate(1)
            aggregate(1)

            def step(b, pair, p):
                if live(b):
                    times_up(b, 0)
                if live(b + 1) and later(b + 1, 2):
                    statistics(b + 1, 1 - p, pair + p)
                if live(b - 1):
                    reciprocal(b - 1, 1 - p)
                if live(b + 1) and later(b + 1, 2):
                    wait_to_aggregate(b + 1)
                if live(b):
                    row_max(b, p, 1)
                if live(b + 1) and later(b + 1, 2):
                    aggregate(1 - p)
                if live(b):
                    row_max(b, p, 0)
                    gate(b, 1)
                    times_up(b, 1)
                if live(b - 1):
                    av_part(b - 1)
                if live(b):
                    row_max(b, p, 3)
                    probsT_part(b, p, 1)
                    row_max(b, p, 2)
                    gate(b, 2)
                if live(b + 1):
                    xT_part(b + 1, 1 - p)
                if live(b):
                    probsT_part(b, p, 0)
                    times_up(b, 2)
                    probsT_part(b, p, 3)
                if live(b - 1):
                    gate_ffn(b - 1)
                if live(b + 1):
                    q_part(b + 1, 1 - p)
                if live(b):
                    probsT_part(b, p, 2)
                if live(b + 1):
                    gate(b + 1, 0)
                if live(b - 1):
                    times_attention(b - 1)

            run_steps(dve, step)

            dve.wait_ge(back_done, BATCHES)
            dve.wait_ge(recip_done, BATCHES)
            for i in range(TILES):
                s = slice(i * D, (i + 1) * D)
                last = nc.vector.scalar_tensor_tensor(out=x_all[:, BATCHES - 1, s], in0=ffn_ps[:, s],
                                                      scalar=recip[1][:, i:i + 1], in1=x_all[:, BATCHES - 1, s],
                                                      op0=ALU.mult, op1=ALU.add)
                if i % (TILES // 2) == TILES // 2 - 1:
                    last.then_inc(last_done, 1)

def kernel(**inputs):
    import numpy as np
    import concourse.bacc as bacc
    from concourse.bass_utils import run_bass_kernel_spmd

    laid_out = {
        "x": np.asarray(inputs["L0_attn_x"]),
        "qk": np.asarray(inputs["L0_attn_QK"]),
        "vo": np.asarray(inputs["L0_attn_VO"]),
        "w_gate_t": np.asarray(inputs["L0_ffn_w_gate"]).T,
        "w_up_t": np.asarray(inputs["L0_ffn_w_up"]).T,
        "w_down_t": np.asarray(inputs["L0_ffn_w_down"]).T,
    }
    nc = bacc.Bacc("TRN2", target_bir_lowering=False, num_devices=1)
    arrays, args = {}, []
    for name, a in laid_out.items():
        a = np.ascontiguousarray(a)
        arrays[f"in_{name}"] = a
        args.append(nc.dram_tensor(f"in_{name}", a.shape, mybir.dt.from_np(a.dtype), kind="ExternalInput").ap())
    args.append(nc.dram_tensor("out_dram", laid_out["x"].shape, F32, kind="ExternalOutput").ap())
    gated_attention_kernel(nc, *args)
    return run_bass_kernel_spmd(nc, [arrays], core_ids=[0]).results[0]["out_dram"]
```
